# Optimizing a Trainium2 kernel written in Bass

```python
import numpy as np
import jax
import jax.numpy as jnp

def _softmax(x, axis=-1):
    return jax.nn.softmax(x, axis=axis)
def _gelu(x):
    return jax.nn.gelu(x, approximate=True)
def _silu(x):
    return jax.nn.silu(x)
def _sigmoid(x):
    return jax.nn.sigmoid(x)
def _layernorm(x, axis=-1, eps=1e-5):
    m = jnp.mean(x, axis=axis, keepdims=True)
    v = jnp.var(x, axis=axis, keepdims=True)
    return (x - m) / jnp.sqrt(v + eps)
def _scatter_add(tgt, idx, src, axis=0):
    return tgt.at[idx].add(src)
def _segment_sum(src, seg, n):
    return jax.ops.segment_sum(src, seg, n)

kernel_name = 'mk_adj_resnorm_d4_adj_128_167b89'

def setup_inputs(seed: int = 0):
    np.random.seed(seed)
    _w = jnp.asarray
    def _rec_inputs():
        import jax
        import jax.numpy as jnp
        _gk = jax.random.key(seed)
        x = -0.0002928 + 1 * jax.random.normal(jax.random.fold_in(_gk, 1), (64, 256, 128), jnp.float32)
        _a = jax.random.bernoulli(jax.random.fold_in(_gk, 2), 0.03125, (256, 256))
        _a = jnp.logical_or(_a, jnp.eye(256, dtype=bool))
        _af = _a.astype(jnp.float32)
        adj = _af
        return x, adj
    x, adj = _rec_inputs()
    def _L0_gnn_setup():
        import jax, jax.numpy as jnp
        import numpy as np
        B, N, D = (4, 8192, 128)
        key = jax.random.key(seed)
        kx, ka, kq, kk, kv = jax.random.split(key, 5)
        x = jax.random.normal(kx, (B, N, D), dtype=jnp.float32)
        mask = (jax.random.uniform(ka, (N, N)) < 0.05).astype(jnp.float32)
        A_shape = jnp.clip(mask + jnp.eye(N, dtype=jnp.float32), 0.0, 1.0)
        q = jax.random.normal(kq, (D, D), dtype=jnp.float32)
        k = jax.random.normal(kk, (D, D), dtype=jnp.float32)
        v = jax.random.normal(kv, (D, D), dtype=jnp.float32)
        return {'x': x, 'A_shape': A_shape, 'q': q, 'k': k, 'v': v}
    _L0_gnn_all = _L0_gnn_setup()
    _L0_gnn_in = {k: v for k, v in _L0_gnn_all.items() if k in ('q', 'k', 'v', )}
    del _L0_gnn_all

    def _L1_gnn_setup():
        import jax, jax.numpy as jnp
        import numpy as np
        B, N, D = (32, 1024, 128)
        TIME_STEP = 5
        key = jax.random.key(seed)
        ks = jax.random.split(key, 12)
        s2 = 1.0 / np.sqrt(2 * D)
        s1 = 1.0 / np.sqrt(D)
        return {'input': jax.random.normal(ks[0], (B, N, D), jnp.float32), 'in_matrix': jax.random.uniform(ks[1], (N, N), jnp.float32), 'out_matrix': jax.random.uniform(ks[2], (N, N), jnp.float32), 'w3_w': jax.random.normal(ks[3], (D, 2 * D), jnp.float32) * s2, 'w3_b': jnp.zeros((D,), jnp.float32), 'u3_w': jax.random.normal(ks[4], (D, D), jnp.float32) * s1, 'u3_b': jnp.zeros((D,), jnp.float32), 'w4_w': jax.random.normal(ks[5], (D, 2 * D), jnp.float32) * s2, 'w4_b': jnp.zeros((D,), jnp.float32), 'w5_w': jax.random.normal(ks[6], (D, 2 * D), jnp.float32) * s2, 'w5_b': jnp.zeros((D,), jnp.float32), 'u5_w': jax.random.normal(ks[7], (D, D), jnp.float32) * s1, 'u5_b': jnp.zeros((D,), jnp.float32), 'time_step': TIME_STEP}
    _L1_gnn_all = _L1_gnn_setup()
    _L1_gnn_in = {k: v for k, v in _L1_gnn_all.items() if k in ('w3_w', 'w3_b', 'u3_w', 'u3_b', 'w4_w', 'w4_b', 'w5_w', 'w5_b', 'u5_w', 'u5_b', )}
    del _L1_gnn_all

    def _L2_gnn_setup():
        import jax, jax.numpy as jnp
        import numpy as np
        from jax import lax
        CONV_ORDER = 3

        def _chebyshev(adj, x, order):

            def step(carry, _):
                nxt = jnp.einsum('ij,bjc->bic', adj, carry)
                return (nxt, nxt)
            _, xs = lax.scan(step, x, None, length=order)
            return jnp.moveaxis(xs, 0, -1)
        key = jax.random.key(seed)
        k1, k2, k3, k4 = jax.random.split(key, 4)
        B, E, C_in, C_out, K, n_adjs = (8, 4096, 128, 128, CONV_ORDER, 2)
        x_1 = jax.random.normal(k1, (B, E, C_in), dtype=jnp.float32)
        adj0 = jax.random.normal(k2, (E, E), dtype=jnp.float32) / np.sqrt(E)
        adj1 = jax.random.normal(k3, (E, E), dtype=jnp.float32) / np.sqrt(E)
        kdim = K * n_adjs + 1
        std = 1.414 * np.sqrt(2.0 / float((C_in + C_out) * kdim))
        weight_1 = std * jax.random.normal(k4, (C_in, C_out, kdim), dtype=jnp.float32)
        return {'x_1': x_1, 'adj0': adj0, 'adj1': adj1, 'weight_1': weight_1}
    _L2_gnn_all = _L2_gnn_setup()
    _L2_gnn_in = {k: v for k, v in _L2_gnn_all.items() if k in ('weight_1', )}
    del _L2_gnn_all

    def _L3_gnn_setup():
        import jax, jax.numpy as jnp
        import numpy as np
        N, D, B = (8192, 128, 2)
        key = jax.random.key(seed)
        ks = jax.random.split(key, 9)
        H = jax.random.normal(ks[0], (B, N, D), dtype=jnp.float32)
        A = jax.random.uniform(ks[1], (N, N), dtype=jnp.float32)
        coeff = jax.random.uniform(ks[2], (N, N), dtype=jnp.float32) / N
        s_d = 1.0 / np.sqrt(D)
        s_2d = 1.0 / np.sqrt(2 * D)
        psi_w = jax.random.normal(ks[3], (D, D), dtype=jnp.float32) * s_d
        psi_b = jnp.zeros((D,), dtype=jnp.float32)
        phi1_w = jax.random.normal(ks[4], (2 * D, D), dtype=jnp.float32) * s_2d
        phi1_b = jnp.zeros((D,), dtype=jnp.float32)
        phi2_w = jax.random.normal(ks[5], (D, D), dtype=jnp.float32) * s_d
        phi2_b = jnp.zeros((D,), dtype=jnp.float32)
        return {'H': H, 'A': A, 'coeff': coeff, 'psi_w': psi_w, 'psi_b': psi_b, 'phi1_w': phi1_w, 'phi1_b': phi1_b, 'phi2_w': phi2_w, 'phi2_b': phi2_b}
    _L3_gnn_all = _L3_gnn_setup()
    _L3_gnn_in = {k: v for k, v in _L3_gnn_all.items() if k in ('psi_w', 'psi_b', 'phi1_w', 'phi1_b', 'phi2_w', 'phi2_b', )}
    del _L3_gnn_all

    return {
        "x": x,
        "adj": adj,
        "L0_gnn_q": _L0_gnn_in["q"],
        "L0_gnn_k": _L0_gnn_in["k"],
        "L0_gnn_v": _L0_gnn_in["v"],
        "L1_gnn_w3_w": _L1_gnn_in["w3_w"],
        "L1_gnn_w3_b": _L1_gnn_in["w3_b"],
        "L1_gnn_u3_w": _L1_gnn_in["u3_w"],
        "L1_gnn_u3_b": _L1_gnn_in["u3_b"],
        "L1_gnn_w4_w": _L1_gnn_in["w4_w"],
        "L1_gnn_w4_b": _L1_gnn_in["w4_b"],
        "L1_gnn_w5_w": _L1_gnn_in["w5_w"],
        "L1_gnn_w5_b": _L1_gnn_in["w5_b"],
        "L1_gnn_u5_w": _L1_gnn_in["u5_w"],
        "L1_gnn_u5_b": _L1_gnn_in["u5_b"],
        "L2_gnn_weight_1": _L2_gnn_in["weight_1"],
        "L3_gnn_psi_w": _L3_gnn_in["psi_w"],
        "L3_gnn_psi_b": _L3_gnn_in["psi_b"],
        "L3_gnn_phi1_w": _L3_gnn_in["phi1_w"],
        "L3_gnn_phi1_b": _L3_gnn_in["phi1_b"],
        "L3_gnn_phi2_w": _L3_gnn_in["phi2_w"],
        "L3_gnn_phi2_b": _L3_gnn_in["phi2_b"],
    }

def reference(x, adj, L0_gnn_q, L0_gnn_k, L0_gnn_v, L1_gnn_w3_w, L1_gnn_w3_b, L1_gnn_u3_w, L1_gnn_u3_b, L1_gnn_w4_w, L1_gnn_w4_b, L1_gnn_w5_w, L1_gnn_w5_b, L1_gnn_u5_w, L1_gnn_u5_b, L2_gnn_weight_1, L3_gnn_psi_w, L3_gnn_psi_b, L3_gnn_phi1_w, L3_gnn_phi1_b, L3_gnn_phi2_w, L3_gnn_phi2_b):
    import jax
    import jax.numpy as jnp
    def _L0_gnn_ref(x, A_shape, q, k, v):
        import jax, jax.numpy as jnp
        import numpy as np
        B, N, D = (4, 8192, 128)
        input_dimension = x.shape[-1]
        Q = x @ q
        K = x @ k
        A = jnp.einsum('bnd,bmd->bnm', Q, K)
        A = A / jnp.sqrt(jnp.float32(input_dimension))
        A = jnp.tanh(A / 8.0) * 8.0
        A = jnp.exp(A) * A_shape
        A = A / jnp.sum(A, axis=-1, keepdims=True)
        out = A @ x @ v
        return out

    def _L1_gnn_ref(input, in_matrix, out_matrix, w3_w, w3_b, u3_w, u3_b, w4_w, w4_b, w5_w, w5_b, u5_w, u5_b, time_step):
        import jax, jax.numpy as jnp
        import numpy as np
        B, N, D = (32, 1024, 128)
        TIME_STEP = 5
        def step(h, _):
            m_in = jnp.einsum('nm,bmd->bnd', in_matrix, h)
            m_out = jnp.einsum('nm,bmd->bnd', out_matrix, h)
            av = jnp.concatenate([m_in, m_out], axis=-1)
            u3 = h @ u3_w.T + u3_b
            z = jax.nn.sigmoid(av @ w3_w.T + w3_b + u3)
            r = jax.nn.sigmoid(av @ w4_w.T + w4_b + u3)
            hv = jnp.tanh(av @ w5_w.T + w5_b + (r * h @ u5_w.T + u5_b))
            h = (1.0 - z) * h + z * hv
            return (h, None)
        h, _ = jax.lax.scan(step, input, None, length=time_step)
        return h

    def _L2_gnn_ref(x_1, adj0, adj1, weight_1):
        import jax, jax.numpy as jnp
        import numpy as np
        from jax import lax
        CONV_ORDER = 3

        def _chebyshev(adj, x, order):

            def step(carry, _):
                nxt = jnp.einsum('ij,bjc->bic', adj, carry)
                return (nxt, nxt)
            _, xs = lax.scan(step, x, None, length=order)
            return jnp.moveaxis(xs, 0, -1)
        parts = [x_1[..., None], _chebyshev(adj0, x_1, CONV_ORDER), _chebyshev(adj1, x_1, CONV_ORDER)]
        x_all = jnp.concatenate(parts, axis=3)
        y_1 = jnp.einsum('bnik,iok->bno', x_all, weight_1)
        return y_1

    def _L3_gnn_ref(H, A, coeff, psi_w, psi_b, phi1_w, phi1_b, phi2_w, phi2_b):
        import jax, jax.numpy as jnp
        import numpy as np
        N, D, B = (8192, 128, 2)
        weights = coeff * A
        features = jax.nn.relu(jnp.einsum('bnd,de->bne', H, psi_w) + psi_b)
        messages = jnp.einsum('nm,bnd->bmd', weights, features)
        phi_in = jnp.concatenate((messages, H), axis=-1)
        h = jax.nn.relu(jnp.einsum('bnk,kd->bnd', phi_in, phi1_w) + phi1_b)
        return jnp.einsum('bnd,de->bne', h, phi2_w) + phi2_b

    x = _layernorm(x + _L0_gnn_ref(x, adj, L0_gnn_q, L0_gnn_k, L0_gnn_v), axis=-1)
    x = _layernorm(x + _L1_gnn_ref(x, adj, adj, L1_gnn_w3_w, L1_gnn_w3_b, L1_gnn_u3_w, L1_gnn_u3_b, L1_gnn_w4_w, L1_gnn_w4_b, L1_gnn_w5_w, L1_gnn_w5_b, L1_gnn_u5_w, L1_gnn_u5_b, 5), axis=-1)
    x = _layernorm(x + _L2_gnn_ref(x, adj, adj, L2_gnn_weight_1), axis=-1)
    x = _layernorm(x + _L3_gnn_ref(x, adj, adj, L3_gnn_psi_w, L3_gnn_psi_b, L3_gnn_phi1_w, L3_gnn_phi1_b, L3_gnn_phi2_w, L3_gnn_phi2_b), axis=-1)
    return x


_drawn_inputs = setup_inputs


def setup_inputs(seed=0):
    import zlib

    import numpy as np

    out = dict(_drawn_inputs(seed))
    spreads = {'L1_gnn_w3_b': (0.0, 0.1),
     'L1_gnn_u3_b': (0.0, 0.1),
     'L1_gnn_w4_b': (0.0, 2.0),
     'L1_gnn_w5_b': (0.0, 0.1),
     'L1_gnn_u5_b': (0.0, 0.1),
     'L3_gnn_psi_b': (0.0, 0.1),
     'L3_gnn_phi1_b': (0.0, 0.327),
     'L3_gnn_phi2_b': (0.0, 0.269)}
    factors = {}
    for name, (base, spread) in spreads.items():
        noise = np.random.default_rng([zlib.crc32(name.encode()), seed]).standard_normal(out[name].shape)
        drawn = base * np.exp(spread * noise) if base else spread * noise
        out[name] = jnp.asarray(drawn.astype(out[name].dtype))
    for name, factor in factors.items():
        out[name] = (out[name] * factor).astype(out[name].dtype)
    return out
```

```python
from contextlib import ExitStack

import concourse.bass as bass
from concourse import mybir

ALU = mybir.AluOpType
ACT = mybir.ActivationFunctionType
F32 = mybir.dt.float32
F32R = mybir.dt.float32r
EPS = 1e-5


def wait_count(eng, sem, count):
    if not isinstance(count, int) or count > 0:
        eng.wait_ge(sem, count)


def adj_resnorm_d4_kernel(nc, t, out):
    BATCHES, N, D = t["x"].shape
    assert D == 128 and N == 256
    KC = N // 128
    GB = 2
    TILES = GB * KC
    COLS = GB * N
    GROUPS = BATCHES // GB
    STEPS = 5
    SCORE = 1.0 / (8.0 * float(D) ** 0.5)

    x_view = t["x"].rearrange("b (c p) d -> p (b c) d", p=128)
    out_view = out.rearrange("b (c p) d -> p (b c) d", p=128)

    with ExitStack() as top:
        def keep(name, shape, dt=F32):
            return top.enter_context(nc.sbuf_tensor(name, shape, dt))

        psum = top.enter_context(nc.psum_tensor("psum", [128, 8, 512], F32))

        state = keep("state", [128, GROUPS * COLS])
        ident = keep("ident", [128, 128])
        adj_n = keep("adj_n", [128, KC, N])
        adj_t = keep("adj_t", [128, KC, N])
        adj_t_hi = keep("adj_t_hi", [128, KC, N], F32R)
        adj_sq_hi = keep("adj_sq_hi", [128, KC, N], F32R)
        qk = keep("qk", [128, D])
        v = keep("v", [128, D])
        w4_hi = keep("w4_hi", [128, D], F32R)
        w4_lo = keep("w4_lo", [128, D], F32R)
        w5_hi = keep("w5_hi", [128, D], F32R)
        w5_lo = keep("w5_lo", [128, D], F32R)
        w34_hi = keep("w34_hi", [128, D], F32R)
        w34_lo = keep("w34_lo", [128, D], F32R)
        u3 = keep("u3", [128, D])
        u5 = keep("u5", [128, D])
        bias_cols = keep("bias_cols", [128, 9])
        wcat = keep("wcat", [128, 4, D])
        psi = keep("psi", [128, D])
        phi1m = keep("phi1m", [128, D])
        phi1x = keep("phi1x", [128, D])
        phi2 = keep("phi2", [128, D])
        ones = keep("ones", [128, 128], F32R)
        psi_row = keep("psi_row", [128, TILES, D], F32R)
        phi2_row = keep("phi2_row", [128, TILES, D], F32R)

        setup(nc, t, psum, locals())
        attention_layer(nc, psum, locals())
        gated_layer(nc, psum, locals())
        graph_conv_layers(nc, psum, locals())


def combine_stats(dve, stats, moments, parts, var_eps, parts_done, terms_done, var_done, n):
    D = 128
    dve.tensor_tensor(moments[:, :, :], stats[:, :, 0:3], stats[:, :, 3:6], ALU.add)
    dve.tensor_tensor(parts[:, 0, :], stats[:, :, 1], stats[:, :, 4], ALU.subtract).then_inc(parts_done, 1)
    dve.wait_ge(parts_done, n + 1)
    dve.tensor_scalar(parts[:, 1, :], moments[:, :, 2], 1.0 / D, EPS, ALU.mult, ALU.add)
    dve.scalar_tensor_tensor(out=parts[:, 2, :], in0=parts[:, 0, :], scalar=0.25, in1=parts[:, 0, :],
                             op0=ALU.mult, op1=ALU.mult)
    dve.tensor_scalar(moments[:, :, 1], moments[:, :, 1], 0.5, None, ALU.mult).then_inc(terms_done, 1)
    dve.wait_ge(terms_done, n + 1)
    dve.tensor_tensor(var_eps, parts[:, 1, :], parts[:, 2, :], ALU.add).then_inc(var_done, 1)


def setup(nc, t, psum, env):
    ident, adj_n, adj_t, adj_t_hi, adj_sq_hi = (env[k] for k in ("ident", "adj_n", "adj_t", "adj_t_hi", "adj_sq_hi"))
    KC, N, D, TILES = env["KC"], env["N"], env["D"], env["TILES"]
    bias_cols, wcat, ones = env["bias_cols"], env["wcat"], env["ones"]
    with ExitStack() as ctx:
        def sb(name, shape, dt=F32):
            return ctx.enter_context(nc.sbuf_tensor(name, shape, dt))

        def sem(name):
            return ctx.enter_context(nc.semaphore(name))

        q_in, k_in = sb("q_in", [128, D]), sb("k_in", [128, D])
        w_in = sb("w_in", [128, 3, 2 * D])
        u_in = sb("u_in", [128, 2, D])
        conv_in = sb("conv_in", [128, D * 7])
        w_sum = sb("w_sum", [128, 3, D])
        w_dif = sb("w_dif", [128, D])
        qk_t = sb("qk_t", [128, 2, D])
        row_in = sb("row_in", [128, 2, D])
        row_hi = sb("row_hi", [128, 2, D], F32R)

        loaded = sem("loaded")
        rows_loaded = sem("rows_loaded")
        ident_zero, ident_done = sem("ident_zero"), sem("ident_done")
        rows_clear = sem("rows_clear")
        w_summed, w_ready = sem("w_summed"), sem("w_ready")
        turned = sem("turned")
        qk_t_done, qk_mm = sem("qk_t_done"), sem("qk_mm")
        hi_done = sem("hi_done")
        row_hi_done = sem("row_hi_done")
        bias_summed = sem("bias_summed")

        loads = [
            (adj_n[:, :, :], t["adj"].rearrange("(c p) m -> p c m", p=128)),
            (q_in[:, :], t["L0_gnn_q"]), (k_in[:, :], t["L0_gnn_k"]), (env["v"][:, :], t["L0_gnn_v"]),
            (w_in[:, 0, :], t["L1_gnn_w3_w"]), (w_in[:, 1, :], t["L1_gnn_w4_w"]), (w_in[:, 2, :], t["L1_gnn_w5_w"]),
            (u_in[:, 0, :], t["L1_gnn_u3_w"]), (u_in[:, 1, :], t["L1_gnn_u5_w"]),
            (conv_in[:, :], t["L2_gnn_weight_1"].rearrange("i o k -> i (o k)")),
            (env["psi"][:, :], t["L3_gnn_psi_w"]),
            (env["phi1m"][:, :], t["L3_gnn_phi1_w"][0:D, :]), (env["phi1x"][:, :], t["L3_gnn_phi1_w"][D:2 * D, :]),
            (env["phi2"][:, :], t["L3_gnn_phi2_w"]),
        ] + [(bias_cols[:, i:i + 1], t[name].rearrange("(p o) -> p o", o=1)) for i, name in enumerate(
            ("L1_gnn_w4_b", "L1_gnn_w3_b", "L1_gnn_w5_b", "L1_gnn_u3_b", "L1_gnn_u5_b", "L3_gnn_phi1_b"))]
        ALL_LOADED = 16 * len(loads)

        block = ctx.enter_context(nc.Block())

        @block.sync
        def _(sp):
            for dst, src in loads:
                sp.dma_start(dst, src).then_inc(loaded, 16)
            sp.wait_ge(rows_clear, 1)
            for i, name in enumerate(("L3_gnn_psi_b", "L3_gnn_phi2_b")):
                for row in (0, 32):
                    sp.dma_start(row_in[row:row + 1, i, :], t[name].rearrange("(o d) -> o d", o=1)).then_inc(rows_loaded, 16)

        @block.gpsimd
        def _(pool):
            pool.memset(row_in[:, :, :], 0.0).then_inc(rows_clear, 1)
            pool.memset(ident[:, :], 0.0).then_inc(ident_zero, 1)
            pool.wait_ge(ident_zero, 1)
            pool.affine_select(out=ident[:, :], in_=ident[:, :], compare_op=ALU.not_equal, fill=1.0, base=0,
                               pattern=[[-1, 128]], channel_multiplier=1).then_inc(ident_done, 1)

        @block.tensor
        def _(pe):
            pe.wait_ge(loaded, ALL_LOADED)
            pe.wait_ge(ident_done, 1)
            for k in range(KC):
                for c in range(KC):
                    mm = pe.transpose(psum[:, 0, k * N + c * 128:k * N + c * 128 + 128],
                                      adj_n[:, c, k * 128:(k + 1) * 128], ident[:, :])
            mm.then_inc(turned, 1)
            pe.transpose(psum[:, 1, 0:D], q_in[:, :], ident[:, :])
            pe.transpose(psum[:, 1, D:2 * D], k_in[:, :], ident[:, :]).then_inc(turned, 1)
            pe.transpose(psum[:, 2, 0:D], u_in[:, 0, :], ident[:, :])
            pe.transpose(psum[:, 2, D:2 * D], u_in[:, 1, :], ident[:, :]).then_inc(turned, 1)
            pe.wait_ge(w_ready, 1)
            for i, w in enumerate((w_sum[:, 0, :], w_sum[:, 1, :], w_dif[:, :])):
                mm = pe.transpose(psum[:, 3, i * D:(i + 1) * D], w, ident[:, :])
            mm.then_inc(turned, 1)
            pe.wait_ge(qk_t_done, 1)
            pe.matmul(psum[:, 4, 0:D], qk_t[:, 0, :], qk_t[:, 1, :], start=True, stop=True).then_inc(qk_mm, 1)

        @block.vector
        def _(dve):
            dve.wait_ge(loaded, ALL_LOADED)
            for i, src in enumerate((1, 2, 0)):
                op = dve.tensor_tensor(w_sum[:, i, :], w_in[:, src, 0:D], w_in[:, src, D:2 * D], ALU.add)
            op.then_inc(w_summed, 1)
            dve.wait_ge(w_summed, 1)
            dve.tensor_tensor(w_dif[:, :], w_sum[:, 2, :], w_sum[:, 0, :], ALU.subtract).then_inc(w_ready, 1)
            dve.tensor_tensor(adj_sq_hi[:, :, :], adj_n[:, :, :], adj_n[:, :, :], ALU.mult)
            by_power = conv_in[:, :].rearrange("p (o k) -> p k o", k=7)
            dve.tensor_copy(wcat[:, 0, :], by_power[:, 0, :])
            for j in range(1, 4):
                dve.tensor_tensor(wcat[:, j, :], by_power[:, j, :], by_power[:, j + 3, :], ALU.add)
            dve.tensor_tensor(bias_cols[:, 6:8], bias_cols[:, 0:2], bias_cols[:, 3:4].broadcast_to([128, 2]), ALU.add)
            dve.tensor_tensor(bias_cols[:, 8:9], bias_cols[:, 2:3], bias_cols[:, 4:5], ALU.add).then_inc(bias_summed, 1)
            dve.memset(ones[:, :].bitcast(F32), 1.0)
            dve.wait_ge(turned, 1)
            dve.tensor_copy(adj_t[:, :, :], psum[:, 0, :].rearrange("p (k n) -> p k n", k=KC))
            dve.tensor_copy(adj_t_hi[:, :, :], psum[:, 0, :].rearrange("p (k n) -> p k n", k=KC))
            dve.wait_ge(turned, 2)
            dve.tensor_copy(qk_t[:, :, :], psum[:, 1, 0:2 * D].rearrange("p (k n) -> p k n", k=2)).then_inc(qk_t_done, 1)
            dve.wait_ge(turned, 3)
            dve.tensor_copy(env["u3"][:, :], psum[:, 2, 0:D])
            dve.tensor_copy(env["u5"][:, :], psum[:, 2, D:2 * D])
            dve.wait_ge(turned, 4)
            for i, w in enumerate(("w4", "w5", "w34")):
                dve.tensor_copy(env[w + "_hi"][:, :], psum[:, 3, i * D:(i + 1) * D]).then_inc(hi_done, 1)
            dve.wait_ge(hi_done, 3)
            for i, w in enumerate(("w4", "w5", "w34")):
                dve.tensor_tensor(env[w + "_lo"][:, :], psum[:, 3, i * D:(i + 1) * D],
                                  env[w + "_hi"][:, :].bitcast(F32), ALU.subtract)
            dve.wait_ge(qk_mm, 1)
            dve.tensor_copy(env["qk"][:, :], psum[:, 4, 0:D])
            dve.wait_ge(rows_loaded, 64)
            dve.tensor_copy(row_hi[:, :, :], row_in[:, :, :]).then_inc(row_hi_done, 1)
            dve.wait_ge(row_hi_done, 1)
            for i, row in enumerate((env["psi_row"], env["phi2_row"])):
                wide = [128, TILES, D]
                dve.tensor_tensor(row[:, :, :], row_in[:, i:i + 1, :].broadcast_to(wide),
                                  row_hi[:, i:i + 1, :].bitcast(F32).broadcast_to(wide), ALU.subtract)\
                   .then_inc(row_hi_done, 1)
            dve.wait_ge(row_hi_done, 3)
            for i, row in enumerate((env["psi_row"], env["phi2_row"])):
                dve.tensor_copy(row[0:1, :, :], row_hi[0:1, i:i + 1, :].bitcast(F32).broadcast_to([1, TILES, D]))


def attention_layer(nc, psum, env):
    KC, N, D, GB, TILES, COLS, GROUPS = (env[k] for k in ("KC", "N", "D", "GB", "TILES", "COLS", "GROUPS"))
    state, ident, adj_t, qk, v, x_view, SCORE = (env[k] for k in ("state", "ident", "adj_t", "qk", "v", "x_view", "SCORE"))
    U = 4
    LAG_OUT, LAG_TURN = 2, 3

    with ExitStack() as ctx:
        def sb(name, shape, dt=F32):
            return ctx.enter_context(nc.sbuf_tensor(name, shape, dt))

        def sem(name):
            return ctx.enter_context(nc.semaphore(name))

        x_in = sb("x_in", [128, U, TILES, D])
        x_t = sb("x_t", [128, 2, COLS])
        p_t = sb("p_t", [128, 2, COLS])
        xv = sb("xv", [128, U, TILES, 132])
        cap = sb("cap", [128, 2 * COLS])
        e = sb("e", [128, U, TILES, N])
        y = sb("y", [128, 2, TILES, D])
        x1 = sb("x1", [128, 2, TILES, D])
        den = sb("den", [128, 2, TILES])
        stats = sb("stats", [128, 2, TILES, 6])
        mv = sb("mv", [128, 2, TILES, 3])
        parts = sb("parts", [128, 2, 3, TILES])
        parts_done = sem("parts_done")
        rstd = sb("rstd", [128, 2, TILES])
        var_eps = sb("var_eps", [128, 2, TILES])
        minus_half = sb("minus_half", [128, TILES])
        half_set, var_done = sem("half_set"), sem("var_done")

        B_XT, B_P, B_X1, B_XV, B_S, B_O = 0, 1, 2, 3, 4, 6

        x_loaded = [sem(f"x_loaded{i}") for i in range(U)]
        ones_set = sem("ones_set")
        xt_mm, p_mm, xv_mm, s_mm, o_mm, x1_mm = (sem(n) for n in ("xt_mm", "p_mm", "xv_mm", "s_mm", "o_mm", "x1_mm"))
        xt_done, pt_done, xv_done, cap_done, exp_done, x1t_done = (
            sem(n) for n in ("xt_done", "pt_done", "xv_done", "cap_done", "exp_done", "x1t_done"))
        e_done, den_done, y_done, stats_done, mv_done, rstd_done, x1_done = (
            sem(n) for n in ("e_done", "den_done", "y_done", "stats_done", "mv_done", "rstd_done", "x1_done"))

        def run(eng, slot, lags):
            for u in range(U):
                slot(0, u)
            with eng.Fori(1, GROUPS // U) as it:
                for u in range(U):
                    slot(it, u)
            for u in range(lags):
                slot(GROUPS // U, u)

        def live(it, u, lag):
            return not isinstance(it, int) or 0 <= it * U + u - lag < GROUPS

        block = ctx.enter_context(nc.Block())

        @block.sync
        def _(sp):
            def slot(it, u):
                s = it * U + u
                wait_count(sp, y_done, s - U + 1)
                sp.dma_start(x_in[:, u, :, :], x_view[:, bass.ds(s * TILES, TILES), :]).then_inc(x_loaded[u], 16)
            run(sp, slot, 0)

        @block.gpsimd
        def _(pool):
            pool.memset(xv[:, :, :, D:D + 1], 1.0).then_inc(ones_set, 1)
            pool.memset(minus_half[:, :], -0.5).then_inc(half_set, 1)
            pool.wait_ge(half_set, 1)

            def slot(it, u):
                n, q = it * U + u, u % 2
                pool.wait_ge(var_done, n + 1)
                pool.tensor_tensor(rstd[:, q, :], var_eps[:, q, :], minus_half[:, :], ALU.pow).then_inc(rstd_done, 1)
            run(pool, slot, 0)

        @block.tensor
        def _(pe):
            def slot(it, u):
                s = it * U + u
                if live(it, u, 0):
                    pe.wait_ge(x_loaded[u], (it + 1) * 16)
                    wait_count(pe, xt_done, s)
                    for i in range(TILES):
                        mm = pe.transpose(psum[:, B_XT, i * 128:(i + 1) * 128], x_in[:, u, i, :], ident[:, :])
                    mm.then_inc(xt_mm, 1)
                if live(it, u, LAG_OUT):
                    n, r = s - LAG_OUT, (u - LAG_OUT) % U
                    pe.wait_ge(e_done, n + 1)
                    pe.wait_ge(xv_done, n + 1)
                    if isinstance(it, int) and n == 0:
                        pe.wait_ge(ones_set, 1)
                    wait_count(pe, y_done, n)
                    for b in range(GB):
                        for c in range(KC):
                            for k in range(KC):
                                mm = pe.matmul(psum[:, B_O + b, c * N:c * N + D + 1],
                                               e[:, r, b * KC + k, c * 128:(c + 1) * 128],
                                               xv[:, r, b * KC + k, 0:D + 1], start=(k == 0), stop=(k == KC - 1))
                    mm.then_inc(o_mm, 1)
                if live(it, u, 0):
                    pe.wait_ge(xt_done, s + 1)
                    wait_count(pe, pt_done, s)
                    pe.matmul(psum[:, B_P, :], qk[:, :], x_t[:, u % 2, :], start=True, stop=True).then_inc(p_mm, 1)
                if live(it, u, LAG_TURN):
                    n = s - LAG_TURN
                    pe.wait_ge(x1_done, n + 1)
                    wait_count(pe, x1t_done, n)
                    for i in range(TILES):
                        mm = pe.transpose(psum[:, B_X1, i * 128:(i + 1) * 128], x1[:, (u - LAG_TURN) % 2, i, :], ident[:, :])
                    mm.then_inc(x1_mm, 1)
                if live(it, u, 0):
                    wait_count(pe, xv_done, s)
                    for i in range(TILES):
                        mm = pe.matmul(psum[:, B_XV, i * D:(i + 1) * D], x_t[:, u % 2, i * 128:(i + 1) * 128], v[:, :],
                                       start=True, stop=True)
                    mm.then_inc(xv_mm, 1)
                    pe.wait_ge(pt_done, s + 1)
                    wait_count(pe, cap_done, s)
                    for b in range(GB):
                        for k in range(KC):
                            i = b * KC + k
                            mm = pe.matmul(psum[:, B_S + b, k * N:(k + 1) * N], x_t[:, u % 2, i * 128:(i + 1) * 128],
                                           p_t[:, u % 2, b * N:(b + 1) * N], start=True, stop=True)
                    mm.then_inc(s_mm, 1)
            run(pe, slot, LAG_TURN)

        @block.scalar
        def _(act):
            def slot(it, u):
                s = it * U + u
                if live(it, u, 0):
                    act.wait_ge(xt_mm, s + 1)
                    wait_count(act, s_mm, s - 1)
                    act.copy(x_t[:, u % 2, :], psum[:, B_XT, :]).then_inc(xt_done, 1)
                    act.wait_ge(p_mm, s + 1)
                    act.copy(p_t[:, u % 2, :], psum[:, B_P, :]).then_inc(pt_done, 1)
                if live(it, u, LAG_TURN):
                    n = s - LAG_TURN
                    act.wait_ge(x1_mm, n + 1)
                    act.copy(state[:, bass.ds(n * COLS, COLS)], psum[:, B_X1, :]).then_inc(x1t_done, 1)
                if live(it, u, 0):
                    act.wait_ge(xv_mm, s + 1)
                    wait_count(act, o_mm, s - U + 1)
                    act.copy(xv[:, u, :, 0:D], psum[:, B_XV, :].rearrange("p (i d) -> p i d", d=D)).then_inc(xv_done, 1)
                    act.wait_ge(s_mm, s + 1)
                    wait_count(act, exp_done, s)
                    act.activation(cap[:, :], psum[:, B_S:B_S + GB, :].rearrange("p b n -> p (b n)"), ACT.Tanh,
                                   scale=SCORE).then_inc(cap_done, 1)
                    act.wait_ge(cap_done, s + 1)
                    act.activation(e[:, u, :, :].rearrange("p i n -> p (i n)"), cap[:, :], ACT.Exp,
                                   scale=8.0).then_inc(exp_done, 1)
            run(act, slot, LAG_TURN)

        @block.vector
        def _(dve):
            def slot(it, u):
                s = it * U + u
                if live(it, u, 0):
                    dve.wait_ge(exp_done, s + 1)
                    eb = e[:, u, :, :].rearrange("p (b k) n -> p b (k n)", b=GB)
                    mask = adj_t[:, :, :].rearrange("p (o k) n -> p o (k n)", o=1).broadcast_to([128, GB, KC * N])
                    dve.tensor_tensor(eb, eb, mask, ALU.mult).then_inc(e_done, 1)
                if live(it, u, LAG_OUT):
                    n, r, q = s - LAG_OUT, (u - LAG_OUT) % U, (u - LAG_OUT) % 2
                    dve.wait_ge(o_mm, n + 1)
                    sums = psum[:, B_O:B_O + GB, :].rearrange("p b (c n) -> p (b c) n", c=KC)
                    dve.reciprocal(den[:, q, :], sums[:, :, D]).then_inc(den_done, 1)
                    dve.wait_ge(den_done, n + 1)
                    for i in range(TILES):
                        op = dve.scalar_tensor_tensor(out=y[:, q, i, :], in0=sums[:, i, 0:D], scalar=den[:, q, i:i + 1],
                                                      in1=x_in[:, r, i, :], op0=ALU.mult, op1=ALU.add)
                    op.then_inc(y_done, 1)
                    dve.wait_ge(y_done, n + 1)
                    for i in range(TILES):
                        op = dve.bn_stats(stats[:, q, i, :], y[:, q, i, :])
                    op.then_inc(stats_done, 1)
                    dve.wait_ge(stats_done, n + 1)
                    combine_stats(dve, stats[:, q, :, :], mv[:, q, :, :], parts[:, q, :, :], var_eps[:, q, :],
                                  parts_done, mv_done, var_done, n)
                    dve.wait_ge(rstd_done, n + 1)
                    wait_count(dve, x1_mm, n - 1)
                    for i in range(TILES):
                        op = dve.tensor_scalar(x1[:, q, i, :], y[:, q, i, :], mv[:, q, i, 1:2], rstd[:, q, i:i + 1],
                                               ALU.subtract, ALU.mult)
                    op.then_inc(x1_done, 1)
            run(dve, slot, LAG_OUT)


def gated_layer(nc, psum, env):
    KC, N, D, GB, TILES, COLS, GROUPS, STEPS = (env[k] for k in ("KC", "N", "D", "GB", "TILES", "COLS", "GROUPS", "STEPS"))
    state, ident, adj_hi, u3, u5, bias = (env[k] for k in ("state", "ident", "adj_t_hi", "u3", "u5", "bias_cols"))
    w4_hi, w4_lo, w5_hi, w5_lo, w34_hi, w34_lo = (env[k] for k in ("w4_hi", "w4_lo", "w5_hi", "w5_lo", "w34_hi", "w34_lo"))
    B_R, B_Z, B_C = bias[:, 6:7], bias[:, 7:8], bias[:, 8:9]
    G = 8
    SETS = GROUPS // G
    SET_SLOTS = STEPS * G
    SLOTS = SETS * SET_SLOTS

    with ExitStack() as ctx:
        def sb(name, shape, dt=F32):
            return ctx.enter_context(nc.sbuf_tensor(name, shape, dt))

        def sem(name):
            return ctx.enter_context(nc.semaphore(name))

        h = sb("h", [128, G, COLS])
        hn_hi = sb("hn_hi", [128, 2, TILES, D], F32R)
        hn_lo = sb("hn_lo", [128, 2, TILES, D], F32R)
        m_hi = sb("m_hi", [128, 2, COLS], F32R)
        m_lo = sb("m_lo", [128, 2, COLS], F32R)
        r = sb("r", [128, 2, COLS])
        rh = sb("rh", [128, 2, COLS])
        z = sb("z", [128, 4, COLS])
        cand = sb("cand", [128, 2, COLS])
        dif = sb("dif", [128, COLS])
        inc = sb("inc", [128, COLS])

        B_HN, B_M, B_CAND, B_GATE = 0, 1, 2, 4

        h_loaded = [sem(f"h_loaded{i}") for i in range(G)]
        hn_mm, m_mm, r_mm, z_mm, c_mm = (sem(n) for n in ("hn_mm", "m_mm", "r_mm", "z_mm", "c_mm"))
        hn_hi_done, hn_lo_done, m_hi_done, m_lo_done, r_done, z_done, c_done = (
            sem(n) for n in ("hn_hi_done", "hn_lo_done", "m_hi_done", "m_lo_done", "r_done", "z_done", "c_done"))
        rh_done, dif_done, inc_done, h_done, state_done = (
            sem(n) for n in ("rh_done", "dif_done", "inc_done", "h_done", "state_done"))

        def run(eng, slot, lags):
            for g in range(G):
                slot(0, g, 0)
            with eng.Fori(G, SET_SLOTS, G) as base:
                for g in range(G):
                    slot(base, g, None)
            with eng.Fori(1, SETS) as k:
                for g in range(G):
                    slot(k * SET_SLOTS, g, k)
                with eng.Fori(G, SET_SLOTS, G) as step:
                    for g in range(G):
                        slot(k * SET_SLOTS + step, g, None)
            for g in range(lags):
                slot(SLOTS, g, None)

        def live(base, g, lag):
            return not isinstance(base, int) or 0 <= base + g - lag < SLOTS

        block = ctx.enter_context(nc.Block())

        @block.sync
        def _(sp):
            for g in range(G):
                sp.dma_start(h[:, g, :], state[:, g * COLS:(g + 1) * COLS]).then_inc(h_loaded[g], 16)
            with sp.Fori(1, SETS) as k:
                for g in range(G):
                    sp.wait_ge(state_done, k * G + (g - G + 1))
                    sp.dma_start(h[:, g, :], state[:, bass.ds((k * G + g) * COLS, COLS)]).then_inc(h_loaded[g], 16)

        @block.gpsimd
        def _(pool):
            with pool.Fori(0, SETS) as k:
                for g in range(G):
                    pool.wait_ge(h_done, k * SET_SLOTS + (SET_SLOTS - G + g + 1))
                    x1h = state[:, bass.ds((k * G + g) * COLS, COLS)]
                    pool.tensor_tensor(x1h, h[:, g, :], x1h, ALU.add).then_inc(state_done, 1)

        @block.tensor
        def _(pe):
            def slot(base, g, k):
                s = base + g
                if live(base, g, 0):
                    if k is not None:
                        pe.wait_ge(h_loaded[g], k * 16 + 16)
                    else:
                        pe.wait_ge(h_done, s - G + 1)
                    wait_count(pe, hn_lo_done, s)
                    for i in range(TILES):
                        mm = pe.transpose(psum[:, B_HN, i * 128:(i + 1) * 128], h[:, g, i * 128:(i + 1) * 128], ident[:, :])
                    mm.then_inc(hn_mm, 1)
                    wait_count(pe, z_done, s - 3)
                    pe.matmul(psum[:, B_GATE + g % 4, :], u3[:, :], h[:, g, :], start=True, stop=False,
                              skip_group_check=True)
                if live(base, g, 1):
                    q = (g - 1) % 2
                    gate = psum[:, B_GATE + (g - 1) % 4, :]
                    pe.wait_ge(m_lo_done, s)
                    pe.matmul(gate, w4_hi[:, :], m_hi[:, q, :], start=False, stop=False, skip_group_check=True)
                    pe.matmul(gate, w4_lo[:, :], m_hi[:, q, :], start=False, stop=False, skip_group_check=True)
                    pe.matmul(gate, w4_hi[:, :], m_lo[:, q, :], start=False, stop=True, skip_group_check=True)\
                      .then_inc(r_mm, 1)
                    wait_count(pe, c_done, s - 2)
                    cb = psum[:, B_CAND + q, :]
                    pe.matmul(cb, w5_hi[:, :], m_hi[:, q, :], start=True, stop=False, skip_group_check=True)
                    pe.matmul(cb, w5_lo[:, :], m_hi[:, q, :], start=False, stop=False, skip_group_check=True)
                    pe.matmul(cb, w5_hi[:, :], m_lo[:, q, :], start=False, stop=False, skip_group_check=True)
                if live(base, g, 0):
                    pe.wait_ge(hn_lo_done, s + 1)
                    wait_count(pe, m_lo_done, s)
                    for b in range(GB):
                        for c in range(KC):
                            i = b * KC + c
                            pe.matmul(psum[:, B_M, b * N:(b + 1) * N], hn_hi[:, g % 2, i, :], adj_hi[:, c, :],
                                      start=(c == 0), stop=False)
                            mm = pe.matmul(psum[:, B_M, b * N:(b + 1) * N], hn_lo[:, g % 2, i, :], adj_hi[:, c, :],
                                           start=False, stop=(c == KC - 1))
                    mm.then_inc(m_mm, 1)
                if live(base, g, 2):
                    pe.wait_ge(rh_done, s - 1)
                    pe.matmul(psum[:, B_CAND + g % 2, :], u5[:, :], rh[:, g % 2, :], start=False, stop=True,
                              skip_group_check=True).then_inc(c_mm, 1)
                if live(base, g, 1):
                    pe.wait_ge(r_done, s)
                    pe.matmul(gate, w34_hi[:, :], m_hi[:, q, :], start=False, stop=False, skip_group_check=True)
                    pe.matmul(gate, w34_lo[:, :], m_hi[:, q, :], start=False, stop=False, skip_group_check=True)
                    pe.matmul(gate, w34_hi[:, :], m_lo[:, q, :], start=False, stop=True, skip_group_check=True)\
                      .then_inc(z_mm, 1)
            run(pe, slot, 2)

        @block.scalar
        def _(act):
            def slot(base, g, k):
                s = base + g
                if live(base, g, 0):
                    act.wait_ge(hn_mm, s + 1)
                    wait_count(act, m_mm, s - 1)
                    act.copy(hn_hi[:, g % 2, :, :].rearrange("p i d -> p (i d)"), psum[:, B_HN, :]).then_inc(hn_hi_done, 1)
                if live(base, g, 1):
                    act.wait_ge(r_mm, s)
                    wait_count(act, rh_done, s - 2)
                    act.activation(r[:, (g - 1) % 2, :], psum[:, B_GATE + (g - 1) % 4, :], ACT.Sigmoid,
                                   bias=B_R).then_inc(r_done, 1)
                if live(base, g, 0):
                    act.wait_ge(m_mm, s + 1)
                    wait_count(act, z_mm, s - 1)
                    act.copy(m_hi[:, g % 2, :], psum[:, B_M, :]).then_inc(m_hi_done, 1)
                if live(base, g, 2):
                    act.wait_ge(c_mm, s - 1)
                    wait_count(act, dif_done, s - 3)
                    act.activation(cand[:, g % 2, :], psum[:, B_CAND + g % 2, :], ACT.Tanh, bias=B_C).then_inc(c_done, 1)
                if live(base, g, 1):
                    act.wait_ge(z_mm, s)
                    wait_count(act, inc_done, s - 4)
                    act.activation(z[:, (g - 1) % 4, :], psum[:, B_GATE + (g - 1) % 4, :], ACT.Sigmoid,
                                   bias=B_Z).then_inc(z_done, 1)
            run(act, slot, 2)

        @block.vector
        def _(dve):
            def slot(base, g, k):
                s = base + g
                if live(base, g, 0):
                    dve.wait_ge(hn_hi_done, s + 1)
                    dve.tensor_tensor(hn_lo[:, g % 2, :, :].rearrange("p i d -> p (i d)"), psum[:, B_HN, :],
                                      hn_hi[:, g % 2, :, :].rearrange("p i d -> p (i d)").bitcast(F32),
                                      ALU.subtract).then_inc(hn_lo_done, 1)
                if live(base, g, 1):
                    dve.wait_ge(r_done, s)
                    wait_count(dve, c_mm, s - 2)
                    dve.tensor_tensor(rh[:, (g - 1) % 2, :], r[:, (g - 1) % 2, :], h[:, (g - 1) % G, :],
                                      ALU.mult).then_inc(rh_done, 1)
                if live(base, g, 0):
                    dve.wait_ge(m_hi_done, s + 1)
                    dve.tensor_tensor(m_lo[:, g % 2, :], psum[:, B_M, :], m_hi[:, g % 2, :].bitcast(F32),
                                      ALU.subtract).then_inc(m_lo_done, 1)
                if live(base, g, 2):
                    hg = h[:, (g - 2) % G, :]
                    dve.wait_ge(c_done, s - 1)
                    wait_count(dve, inc_done, s - 2)
                    dve.tensor_tensor(dif[:, :], cand[:, g % 2, :], hg, ALU.subtract).then_inc(dif_done, 1)
                    dve.wait_ge(dif_done, s - 1)
                    dve.wait_ge(z_done, s - 1)
                    wait_count(dve, h_done, s - 2)
                    dve.tensor_tensor(inc[:, :], dif[:, :], z[:, (g - 2) % 4, :], ALU.mult).then_inc(inc_done, 1)
                    dve.wait_ge(inc_done, s - 1)
                    dve.tensor_tensor(hg, hg, inc[:, :], ALU.add).then_inc(h_done, 1)
            run(dve, slot, 2)


def graph_conv_layers(nc, psum, env):
    KC, N, D, GB, TILES, COLS, GROUPS = (env[k] for k in ("KC", "N", "D", "GB", "TILES", "COLS", "GROUPS"))
    state, ident, adj_hi, adj_sq, wcat = (env[k] for k in ("state", "ident", "adj_t_hi", "adj_sq_hi", "wcat"))
    psi, phi1m, phi1x, phi2, ones = (env[k] for k in ("psi", "phi1m", "phi1x", "phi2", "ones"))
    psi_row, phi2_row, out_view = env["psi_row"], env["phi2_row"], env["out_view"]
    B_PHI1 = env["bias_cols"][:, 5:6]
    U = 4

    with ExitStack() as ctx:
        def sb(name, shape, dt=F32):
            return ctx.enter_context(nc.sbuf_tensor(name, shape, dt))

        def sem(name):
            return ctx.enter_context(nc.semaphore(name))

        y1t = sb("y1t", [128, 2, COLS])
        x2 = sb("x2", [128, 2, TILES, D])
        x2t = sb("x2t", [128, COLS])
        c_hi = sb("c_hi", [128, 3, TILES, D], F32R)
        c_lo = sb("c_lo", [128, 3, TILES, D], F32R)
        y2 = sb("y2", [128, TILES, D])
        x3 = sb("x3", [128, 4, TILES, D])
        x3t = sb("x3t", [128, 2, COLS])
        f_hi = sb("f_hi", [128, 2, TILES, D], F32R)
        f_lo = sb("f_lo", [128, 2, TILES, D], F32R)
        msg = sb("msg", [128, COLS])
        hid = sb("hid", [128, COLS])
        y3 = sb("y3", [128, TILES, D])
        res = sb("res", [128, 2, TILES, D])
        stats = sb("c_stats", [128, 3, TILES, 6])
        mv = sb("c_mv", [128, 3, TILES, 3])
        parts = sb("c_parts", [128, 3, 3, TILES])
        parts_done = [sem(f"c_parts_done{i}") for i in range(3)]
        rstd = sb("c_rstd", [128, 3, TILES])
        var_eps = sb("c_var_eps", [128, 3, TILES])
        minus_half = sb("c_minus_half", [128, TILES])
        half_set = sem("c_half_set")

        B_CONV, B_T, B_X2T, B_F, B_MSG = 0, 4, 5, 6, 7

        y1_loaded = [sem(f"y1_loaded{i}") for i in range(2)]
        res_out = [sem(f"res_out{i}") for i in range(2)]
        y1_mm, x2t_mm, x3t_mm, g_mm, f_mm, msg_mm, hid_mm, o_mm = (
            sem("c_" + n) for n in ("y1_mm", "x2t_mm", "x3t_mm", "g_mm", "f_mm", "msg_mm", "hid_mm", "o_mm"))
        a_mm = [sem(f"a_mm{i}") for i in range(3)]
        c_hi_done = [sem(f"c_hi_done{i}") for i in range(3)]
        c_lo_done = [sem(f"c_lo_done{i}") for i in range(3)]
        x2t_done, x3t_done, f_hi_done, f_lo_done, msg_done, hid_done = (
            sem("c_" + n) for n in ("x2t_done", "x3t_done", "f_hi_done", "f_lo_done", "msg_done", "hid_done"))
        y2_done, y3_done, x2_done, x3_done, res_done = (
            sem("c_" + n) for n in ("y2_done", "y3_done", "x2_done", "x3_done", "res_done"))
        stats_done = [sem(f"stats_done{i}") for i in range(3)]
        mv_done = [sem(f"mv_done{i}") for i in range(3)]
        var_done = [sem(f"c_var_done{i}") for i in range(3)]
        rstd_done = [sem(f"rstd_done{i}") for i in range(3)]

        def run(eng, slot, lags, peeled=1):
            for it in range(peeled):
                for u in range(U):
                    slot(it, u)
            with eng.Fori(peeled, GROUPS // U) as it:
                for u in range(U):
                    slot(it, u)
            for u in range(lags):
                slot(GROUPS // U, u)

        def live(it, u, lag):
            return not isinstance(it, int) or 0 <= it * U + u - lag < GROUPS

        def flat(ap):
            return ap.rearrange("p i d -> p (i d)")

        conv = psum[:, B_CONV:B_CONV + TILES, :]

        block = ctx.enter_context(nc.Block())

        @block.sync
        def _(sp):
            def slot(it, u):
                s = it * U + u
                if live(it, u, 0):
                    wait_count(sp, y1_mm, s - 1)
                    sp.dma_start(y1t[:, u % 2, :], state[:, bass.ds(s * COLS, COLS)]).then_inc(y1_loaded[u % 2], 16)
                if live(it, u, 4):
                    n = s - 4
                    sp.wait_ge(res_done, n + 1)
                    sp.dma_start(out_view[:, bass.ds(n * TILES, TILES), :], res[:, u % 2, :, :]).then_inc(res_out[u % 2], 16)
            run(sp, slot, 4)
            for i in range(2):
                sp.wait_ge(res_out[i], GROUPS // 2 * 16)

        @block.gpsimd
        def _(pool):
            pool.memset(minus_half[:, :], -0.5).then_inc(half_set, 1)
            pool.wait_ge(half_set, 1)

            def deviation(which, n):
                pool.wait_ge(var_done[which], n + 1)
                pool.tensor_tensor(rstd[:, which, :], var_eps[:, which, :], minus_half[:, :], ALU.pow)\
                    .then_inc(rstd_done[which], 1)

            def slot(it, u):
                s = it * U + u
                if live(it, u, 2):
                    deviation(1, s - 2)
                if live(it, u, 4):
                    deviation(2, s - 4)
                if live(it, u, 0):
                    deviation(0, s)
            run(pool, slot, 4)

        @block.tensor
        def _(pe):
            def spread(s, lag, level):
                n = s - lag
                pe.wait_ge(c_lo_done[level], n + 1)
                for b in range(GB):
                    for c in range(KC):
                        dst = psum[:, B_CONV + b * KC + c, (2 - level) * D:(3 - level) * D]
                        for k in range(KC):
                            lhs = adj_hi[:, k, c * 128:(c + 1) * 128]
                            pe.matmul(dst, lhs, c_hi[:, level, b * KC + k, :], start=False, stop=False,
                                      skip_group_check=True)
                            mm = pe.matmul(dst, lhs, c_lo[:, level, b * KC + k, :], start=False, stop=(k == KC - 1),
                                           skip_group_check=True)
                mm.then_inc(a_mm[level], 1)

            def slot(it, u):
                s = it * U + u
                if live(it, u, 1):
                    pe.wait_ge(x2_done, s)
                    wait_count(pe, x2t_done, s - 1)
                    for i in range(TILES):
                        mm = pe.transpose(psum[:, B_X2T, i * 128:(i + 1) * 128], x2[:, (u - 1) % 2, i, :], ident[:, :])
                    mm.then_inc(x2t_mm, 1)
                if live(it, u, 3):
                    n, q = s - 3, (u - 3) % 2
                    pe.wait_ge(f_lo_done, n + 1)
                    wait_count(pe, y3_done, n)
                    for b in range(GB):
                        for k in range(KC):
                            i = b * KC + k
                            pe.matmul(psum[:, B_MSG, b * N:(b + 1) * N], f_hi[:, q, i, :], adj_sq[:, k, :],
                                      start=(k == 0), stop=False)
                            mm = pe.matmul(psum[:, B_MSG, b * N:(b + 1) * N], f_lo[:, q, i, :], adj_sq[:, k, :],
                                           start=False, stop=(k == KC - 1))
                    mm.then_inc(msg_mm, 1)
                if live(it, u, 1):
                    pe.wait_ge(x2t_done, s)
                    wait_count(pe, y2_done, s - 1)
                    for i in range(TILES):
                        mm = pe.matmul(psum[:, B_CONV + i, :], x2t[:, i * 128:(i + 1) * 128],
                                       wcat[:, :, :].rearrange("p j d -> p (j d)"), start=True, stop=False,
                                       skip_group_check=True)
                    mm.then_inc(g_mm, 1)
                if live(it, u, 2):
                    n = s - 2
                    pe.wait_ge(x3_done, n + 1)
                    wait_count(pe, x3t_done, n)
                    wait_count(pe, x2_done, n + 2 if live(it, u, 1) else GROUPS)
                    for i in range(TILES):
                        mm = pe.transpose(psum[:, B_T, i * 128:(i + 1) * 128], x3[:, (u - 2) % 4, i, :], ident[:, :])
                    mm.then_inc(x3t_mm, 1)
                if live(it, u, 3):
                    n, q = s - 3, (u - 3) % 2
                    pe.wait_ge(msg_done, n + 1)
                    wait_count(pe, f_lo_done, n + 1)
                    pe.matmul(psum[:, B_F, :], phi1x[:, :], x3t[:, q, :], start=True, stop=False)
                    pe.matmul(psum[:, B_F, :], phi1m[:, :], msg[:, :], start=False, stop=True).then_inc(hid_mm, 1)
                if live(it, u, 1):
                    spread(s, 1, 0)
                if live(it, u, 2):
                    n, q = s - 2, (u - 2) % 2
                    pe.wait_ge(x3t_done, n + 1)
                    wait_count(pe, hid_done, n)
                    pe.matmul(psum[:, B_F, :], ones[:, :], flat(psi_row[:, :, :]), start=True, stop=False,
                              skip_group_check=True)
                    for i in range(TILES):
                        mm = pe.matmul(psum[:, B_F, i * D:(i + 1) * D], x3t[:, q, i * 128:(i + 1) * 128], psi[:, :],
                                       start=False, stop=True, skip_group_check=True)
                    mm.then_inc(f_mm, 1)
                if live(it, u, 0):
                    pe.wait_ge(y1_loaded[u % 2], it * (16 * U // 2) + 16 * (u // 2 + 1))
                    wait_count(pe, x2_done, s)
                    wait_count(pe, x3t_done, s - 1)
                    for i in range(TILES):
                        mm = pe.transpose(psum[:, B_T, i * 128:(i + 1) * 128], y1t[:, u % 2, i * 128:(i + 1) * 128],
                                          ident[:, :])
                    mm.then_inc(y1_mm, 1)
                if live(it, u, 1):
                    spread(s, 1, 1)
                if live(it, u, 3):
                    n = s - 3
                    pe.wait_ge(hid_done, n + 1)
                    pe.wait_ge(msg_done, n + 1)
                    pe.matmul(psum[:, B_MSG, :], ones[:, :], flat(phi2_row[:, :, :]), start=True, stop=False,
                              skip_group_check=True)
                    for i in range(TILES):
                        mm = pe.matmul(psum[:, B_MSG, i * D:(i + 1) * D], hid[:, i * 128:(i + 1) * 128], phi2[:, :],
                                       start=False, stop=True, skip_group_check=True)
                    mm.then_inc(o_mm, 1)
                if live(it, u, 1):
                    spread(s, 1, 2)
            run(pe, slot, 3)

        @block.scalar
        def _(act):
            def inner_hi(s, level, ready):
                act.wait_ge(ready, s)
                wait_count(act, a_mm[level], s - 1)
                act.copy(c_hi[:, level, :, :], conv[:, :, (3 - level) * D:(4 - level) * D]).then_inc(c_hi_done[level], 1)

            def slot(it, u):
                s = it * U + u
                if live(it, u, 1):
                    act.wait_ge(x2t_mm, s)
                    wait_count(act, g_mm, s - 1)
                    act.copy(x2t[:, :], psum[:, B_X2T, :]).then_inc(x2t_done, 1)
                if live(it, u, 3):
                    act.wait_ge(msg_mm, s - 2)
                    wait_count(act, hid_mm, s - 3)
                    act.copy(msg[:, :], psum[:, B_MSG, :]).then_inc(msg_done, 1)
                if live(it, u, 1):
                    inner_hi(s, 0, g_mm)
                if live(it, u, 2):
                    act.wait_ge(x3t_mm, s - 1)
                    wait_count(act, hid_mm, s - 3)
                    act.copy(x3t[:, (u - 2) % 2, :], psum[:, B_T, :]).then_inc(x3t_done, 1)
                if live(it, u, 3):
                    act.wait_ge(hid_mm, s - 2)
                    wait_count(act, o_mm, s - 3)
                    act.activation(hid[:, :], psum[:, B_F, :], ACT.Relu, bias=B_PHI1).then_inc(hid_done, 1)
                if live(it, u, 1):
                    inner_hi(s, 1, a_mm[0])
                if live(it, u, 2):
                    act.wait_ge(f_mm, s - 1)
                    wait_count(act, msg_mm, s - 3)
                    act.activation(flat(f_hi[:, (u - 2) % 2, :, :]), psum[:, B_F, :], ACT.Relu).then_inc(f_hi_done, 1)
                if live(it, u, 1):
                    inner_hi(s, 2, a_mm[1])
            run(act, slot, 3)

        @block.vector
        def _(dve):
            def inner_lo(s, level):
                dve.wait_ge(c_hi_done[level], s)
                dve.tensor_tensor(c_lo[:, level, :, :], conv[:, :, (3 - level) * D:(4 - level) * D],
                                  c_hi[:, level, :, :].bitcast(F32), ALU.subtract).then_inc(c_lo_done[level], 1)

            def normalise(which, n, src, dst, done):
                for i in range(TILES):
                    op = dve.bn_stats(stats[:, which, i, :], src[:, i, :])
                op.then_inc(stats_done[which], 1)
                dve.wait_ge(stats_done[which], n + 1)
                combine_stats(dve, stats[:, which, :, :], mv[:, which, :, :], parts[:, which, :, :], var_eps[:, which, :],
                              parts_done[which], mv_done[which], var_done[which], n)
                dve.wait_ge(rstd_done[which], n + 1)
                for i in range(TILES):
                    op = dve.tensor_scalar(dst[:, i, :], src[:, i, :], mv[:, which, i, 1:2], rstd[:, which, i:i + 1],
                                           ALU.subtract, ALU.mult)
                op.then_inc(done, 1)

            def slot(it, u):
                s = it * U + u
                if live(it, u, 4):
                    n = s - 4
                    dve.wait_ge(o_mm, n + 1)
                    wait_count(dve, res_done, n)
                    dve.tensor_tensor(y3[:, :, :], psum[:, B_MSG, :].rearrange("p (i d) -> p i d", d=D),
                                      x3[:, (u - 4) % 4, :, :], ALU.add).then_inc(y3_done, 1)
                if live(it, u, 2):
                    n = s - 2
                    dve.wait_ge(a_mm[2], n + 1)
                    wait_count(dve, x3_done, n)
                    dve.tensor_tensor(y2[:, :, :], conv[:, :, 0:D], x2[:, (u - 2) % 2, :, :], ALU.add).then_inc(y2_done, 1)
                    dve.wait_ge(y2_done, n + 1)
                    normalise(1, n, y2, x3[:, (u - 2) % 4, :, :], x3_done)
                if live(it, u, 1):
                    inner_lo(s, 0)
                if live(it, u, 4):
                    n = s - 4
                    dve.wait_ge(y3_done, n + 1)
                    if not isinstance(it, int) or n >= 2:
                        dve.wait_ge(res_out[u % 2], it * (16 * U // 2) + (16 * (u // 2) - 16 * U // 2))
                    normalise(2, n, y3, res[:, (u - 4) % 2, :, :], res_done)
                if live(it, u, 1):
                    inner_lo(s, 1)
                if live(it, u, 2):
                    n = s - 2
                    dve.wait_ge(f_hi_done, n + 1)
                    dve.scalar_tensor_tensor(out=flat(f_lo[:, (u - 2) % 2, :, :]), in0=psum[:, B_F, :], scalar=0.0,
                                             in1=flat(f_hi[:, (u - 2) % 2, :, :]).bitcast(F32), op0=ALU.max,
                                             op1=ALU.subtract).then_inc(f_lo_done, 1)
                if live(it, u, 1):
                    inner_lo(s, 2)
                if live(it, u, 0):
                    dve.wait_ge(y1_mm, s + 1)
                    wait_count(dve, x2t_mm, s - 1)
                    normalise(0, s, psum[:, B_T, :].rearrange("p (i d) -> p i d", d=D), x2[:, u % 2, :, :], x2_done)
            run(dve, slot, 4, peeled=2)


_INS = ["x", "adj", "L0_gnn_q", "L0_gnn_k", "L0_gnn_v", "L1_gnn_w3_w", "L1_gnn_w3_b", "L1_gnn_u3_w", "L1_gnn_u3_b",
        "L1_gnn_w4_w", "L1_gnn_w4_b", "L1_gnn_w5_w", "L1_gnn_w5_b", "L1_gnn_u5_w", "L1_gnn_u5_b", "L2_gnn_weight_1",
        "L3_gnn_psi_w", "L3_gnn_psi_b", "L3_gnn_phi1_w", "L3_gnn_phi1_b", "L3_gnn_phi2_w", "L3_gnn_phi2_b"]


def kernel(**inputs):
    import numpy as _np
    import concourse.bacc as _bacc
    from concourse import mybir as _mybir
    from concourse.bass_utils import run_bass_kernel_spmd as _run

    nc = _bacc.Bacc("TRN2", target_bir_lowering=False, num_devices=1)
    arrays, args = {}, {}
    for name in _INS:
        a = _np.ascontiguousarray(inputs[name])
        arrays[f"in_{name}_dram"] = a
        args[name] = nc.dram_tensor(f"in_{name}_dram", a.shape, _mybir.dt.from_np(a.dtype), kind="ExternalInput").ap()
    shape = inputs["x"].shape
    out = nc.dram_tensor("out_dram", shape, _mybir.dt.float32, kind="ExternalOutput").ap()
    adj_resnorm_d4_kernel(nc, args, out)
    r = _run(nc, [arrays], core_ids=[0])
    return r.results[0]["out_dram"]
```
